# Optimizing a Trainium2 kernel written in Bass

```python
import numpy as np
import jax
import jax.numpy as jnp

def _softmax(x, axis=-1):
    return jax.nn.softmax(x, axis=axis)

def _gelu(x):
    return jax.nn.gelu(x, approximate=True)

def _silu(x):
    return jax.nn.silu(x)

def _sigmoid(x):
    return jax.nn.sigmoid(x)

def _layernorm(x, axis=-1, eps=1e-05):
    m = jnp.mean(x, axis=axis, keepdims=True)
    v = jnp.var(x, axis=axis, keepdims=True)
    return (x - m) / jnp.sqrt(v + eps)

def _scatter_add(tgt, idx, src, axis=0):
    return tgt.at[idx].add(src)

def _segment_sum(src, seg, n):
    return jax.ops.segment_sum(src, seg, n)
kernel_name = 'mk_adj_preln_d1_adj_r2_ccd68d'

def setup_inputs(seed: int=0):
    np.random.seed(seed)
    _w = jnp.asarray

    def _rec_inputs():
        import jax
        import jax.numpy as jnp
        _gk = jax.random.key(seed)
        x = -9.806e-05 + 1 * jax.random.normal(jax.random.fold_in(_gk, 1), (4096, 64), jnp.float32)
        _a = jax.random.bernoulli(jax.random.fold_in(_gk, 2), 0.00390625, (4096, 4096))
        _a = jnp.logical_or(_a, jnp.swapaxes(_a, -1, -2))
        _a = jnp.logical_or(_a, jnp.eye(4096, dtype=bool))
        _af = _a.astype(jnp.float32)
        adj = _af
        return (x, adj)
    x, adj = _rec_inputs()

    def _L0_gnn_setup():
        import jax, jax.numpy as jnp
        import numpy as np
        N, D_IN, D_OUT = (4096, 64, 64)
        MAX_NEIGH = 100
        DECAY = 0.5
        key = jax.random.key(seed)
        k1, k2, k3, k4 = jax.random.split(key, 4)
        stdv = 1.0 / np.sqrt(D_OUT)
        inputs = {'input': jax.random.normal(k1, (N, D_IN), dtype=jnp.float32), 'adj': jax.random.randint(k2, (N, N), 0, 2).astype(jnp.float32), 'weight': jax.random.uniform(k3, (D_IN, D_OUT), minval=-stdv, maxval=stdv, dtype=jnp.float32), 'bias': jax.random.uniform(k4, (D_OUT,), minval=-stdv, maxval=stdv, dtype=jnp.float32)}
        return inputs
    _L0_gnn_all = _L0_gnn_setup()
    _L0_gnn_in = {k: v for k, v in _L0_gnn_all.items() if k in ('weight', 'bias')}
    del _L0_gnn_all
    return {'x': x, 'adj': adj, 'L0_gnn_weight': _L0_gnn_in['weight'], 'L0_gnn_bias': _L0_gnn_in['bias']}

def reference(x, adj, L0_gnn_weight, L0_gnn_bias):
    import jax
    import jax.numpy as jnp

    def _L0_gnn_ref(input, adj, weight, bias):
        import jax, jax.numpy as jnp
        import numpy as np
        N, D_IN, D_OUT = (4096, 64, 64)
        MAX_NEIGH = 100
        DECAY = 0.5
        support = input @ weight
        mask = (adj != 0).astype(support.dtype)
        rank = jnp.cumsum(mask, axis=1)
        deg = rank[:, -1:]
        k = jnp.minimum(deg, float(MAX_NEIGH))
        pos = rank - (deg - k)
        w = mask * jnp.where(pos > 0, DECAY ** (k - pos), 0.0)
        out = w @ support + bias
        return out
    h = jnp.maximum(_layernorm(x, axis=-1), 0.0)
    x = x + _L0_gnn_ref(h, adj, L0_gnn_weight, L0_gnn_bias)
    return x

_drawn_inputs = setup_inputs


def setup_inputs(seed=0):
    import zlib

    import numpy as np

    out = dict(_drawn_inputs(seed))
    spreads = {}
    factors = {}
    for name, (base, spread) in spreads.items():
        noise = np.random.default_rng([zlib.crc32(name.encode()), seed]).standard_normal(out[name].shape)
        drawn = base * np.exp(spread * noise) if base else spread * noise
        out[name] = jnp.asarray(drawn.astype(out[name].dtype))
    for name, factor in factors.items():
        out[name] = (out[name] * factor).astype(out[name].dtype)
    return out
```

```python
from contextlib import ExitStack

import concourse.bass as bass
from concourse import mybir

F32 = mybir.dt.float32
BF16 = mybir.dt.bfloat16
I16 = mybir.dt.int16
ALU = mybir.AluOpType
ACT = mybir.ActivationFunctionType
AX_X = mybir.AxisListType.X

P = 128
RT = 4
PANELS = 4
MAX_NEIGH = 100
EPS = 1e-5
EXP_BITS = 128
SHIFT = 127 - MAX_NEIGH
OFF = 8192.0

BITS0 = EXP_BITS * (MAX_NEIGH - OFF)


def gnn_layer(nc, x, adj, weight, bias, out):
    N, D = x.shape
    NT = N // P
    BI = RT * P
    NB = N // BI
    NPAIR = NT // 2
    PC = N // PANELS
    PPP = NPAIR // PANELS
    LNG = 4
    GT = NT // LNG
    SP3 = 3 * D

    adj_v = adj.rearrange("(b t p) c -> b p t c", t=RT, p=P)
    out_v = out.rearrange("(b t p) d -> b p t d", t=RT, p=P)
    x_v = x.rearrange("(t p) d -> p t d", p=P)

    with ExitStack() as ctx:
        def sb(name, shape, dt):
            return ctx.enter_context(nc.sbuf_tensor(name, shape, dt))

        def psum(name, shape, dt):
            return ctx.enter_context(nc.psum_tensor(name, shape, dt))

        def sem(name):
            return ctx.enter_context(nc.semaphore(name))

        panel = sb("panel", [P, PANELS, RT, PC], F32)
        panel_hi = panel[:].rearrange("p q t c -> p (q t c)").bitcast(BF16).rearrange(
            "p (q t c h) -> p q t c h", q=PANELS, t=RT, h=2)[:, :, :, :, 1]
        mask = sb("mask", [P, 4, 2, BI], BF16)
        later = sb("later", [P, 4, 2, BI], BF16)
        wts = sb("wts", [P, 4, 2, BI], I16)
        wts_bf = wts[:].rearrange("p r k i -> p (r k i)").bitcast(BF16).rearrange(
            "p (r k i) -> p r k i", r=4, k=2)
        supp = sb("supp", [P, NT, 3, D], BF16)
        ident = sb("ident", [P, P], BF16)
        ident_f = sb("ident_f", [P, P], F32)
        tri = sb("tri", [P, P], BF16)
        ones = sb("ones", [P, P], BF16)
        wsb = sb("wsb", [D, D], F32)
        bias_sb = sb("bias_sb", [P, D], F32)
        xs = sb("xs", [P, NT, D], F32)
        xb = sb("xb", [P, NT, D], F32)
        xc = sb("xc", [P, NT, D], F32)
        hn = sb("hn", [P, NT, D], F32)
        hT = sb("hT", [D, GT * P], F32)
        s_f = sb("s_f", [P, GT, D], F32)
        s_r = sb("s_r", [P, GT, D], F32)
        stat = sb("stat", [P, 6, NT], F32)
        agg = sb("agg", [P, RT, SP3], F32)
        part = sb("part", [P, 2, RT, D], F32)
        res = sb("res", [P, RT, D], F32)

        ps_t = psum("ps_t", [P, 2, 2, BI], BF16)
        ps_c = psum("ps_c", [P, 2, 2, BI], F32)
        ps_o = psum("ps_o", [P, 2, 512], F32)
        ps_h = ps_c[0:D, 0, :, :].rearrange("p k i -> p (k i)")
        ps_s = ps_c[:, 1, 0, :].rearrange("p (t d) -> p t d", t=GT)

        panel_in = [sem(f"panel_in{q}") for q in range(PANELS)]
        x_in = sem("x_in")
        w_in = sem("w_in")
        bias_in = sem("bias_in")
        consts_step = sem("consts_step")
        ln_step = sem("ln_step")
        ln_var = sem("ln_var")
        ln_sqrt = sem("ln_sqrt")
        h_ready = sem("h_ready")
        h_turned = sem("h_turned")
        hT_ready = sem("hT_ready")
        s_product = sem("s_product")
        s_ready = sem("s_ready")
        xb_ready = sem("xb_ready")
        turned = sem("turned")
        masked = sem("masked")
        summed = sem("summed")
        counted = sem("counted")
        weighed = sem("weighed")
        gathered = sem("gathered")
        agg_ready = sem("agg_ready")
        add_step = sem("add_step")
        res_ready = sem("res_ready")
        stored = sem("stored")

        SUMS = 2 * NPAIR - 2
        CONSTS = 5

        block = ctx.enter_context(nc.Block())

        @block.sync
        def _(sp):
            def load(b, q):
                c0 = N - (q + 1) * PC
                sp.dma_start(panel[:, q], adj_v[b, :, :, c0:c0 + PC]).then_inc(panel_in[q], 16)

            sp.dma_start(xs[:], x_v).then_inc(x_in, 16)
            for q in range(PANELS):
                load(0, q)
            for b in range(1, NB):
                for q in range(PANELS):
                    sp.wait_ge(turned, (b - 1) * NPAIR + (q + 1) * PPP)
                    load(b, q)
                sp.wait_ge(res_ready, b)
                sp.dma_start(out_v[b - 1], res[:]).then_inc(stored, 16)
            sp.wait_ge(res_ready, NB)
            sp.dma_start(out_v[NB - 1], res[:]).then_inc(stored, 16)
            sp.wait_ge(stored, 16 * NB)

        @block.gpsimd
        def _(pool):
            done = [0]

            def link(ins):
                done[0] += 1
                ins.then_inc(consts_step, 1)
                pool.wait_ge(consts_step, done[0])

            pool.dma_start(wsb[:], weight).then_inc(w_in, 16)
            pool.dma_start(bias_sb[:], bias.partition_broadcast(P)).then_inc(bias_in, 16)
            link(nc.gpsimd.memset(ones[:], 1.0))
            link(nc.gpsimd.affine_select(out=tri[:], in_=ones[:], compare_op=ALU.is_gt, fill=0.0, base=0,
                                         pattern=[[-1, P]], channel_multiplier=1))
            link(nc.gpsimd.affine_select(out=tri[:], in_=tri[:], compare_op=ALU.not_equal, fill=-OFF, base=0,
                                         pattern=[[-1, P]], channel_multiplier=1))
            link(nc.gpsimd.affine_select(out=ident[:], in_=ones[:], compare_op=ALU.is_equal, fill=0.0, base=0,
                                         pattern=[[-1, P]], channel_multiplier=1))
            link(nc.gpsimd.affine_select(out=ident_f[:], in_=ones[:], compare_op=ALU.is_equal, fill=0.0, base=0,
                                         pattern=[[-1, P]], channel_multiplier=1))
            pool.wait_ge(bias_in, 16)
            pool.wait_ge(x_in, 16)
            nc.gpsimd.tensor_tensor(
                xb[:], xs[:], bias_sb[:].rearrange("p (a d) -> p a d", a=1).to_broadcast([P, NT, D]),
                ALU.add).then_inc(xb_ready, 1)
            pool.wait_ge(xb_ready, 1)

            def finish(b, first):
                pool.wait_ge(agg_ready, b + 1)
                nc.gpsimd.tensor_tensor(part[:, 0], agg[:, :, 2 * D:3 * D], agg[:, :, D:2 * D],
                                        ALU.add).then_inc(add_step, 1)
                pool.wait_ge(add_step, b * 2 + 1)
                nc.gpsimd.tensor_tensor(part[:, 1], part[:, 0], agg[:, :, 0:D], ALU.add).then_inc(add_step, 1)
                pool.wait_ge(add_step, b * 2 + 2)
                if not first:
                    pool.wait_ge(stored, b * 16)
                nc.gpsimd.tensor_tensor(res[:], part[:, 1], xb[:, bass.ds(b * RT, RT), :],
                                        ALU.add).then_inc(res_ready, 1)

            finish(0, True)
            with pool.Fori(1, NB) as b:
                finish(b, False)

        @block.scalar
        def _(act):
            for g in range(LNG):
                t0 = NT - (g + 1) * GT
                act.wait_ge(ln_var, g + 1)
                nc.scalar.activation(stat[:, 3, t0:t0 + GT], stat[:, 2, t0:t0 + GT], ACT.Sqrt).then_inc(ln_sqrt, 1)
            for g in range(LNG):
                act.wait_ge(h_turned, g + 1)
                if g >= 1:
                    act.wait_ge(s_product, g)
                nc.scalar.copy(hT[:], ps_h).then_inc(hT_ready, 1)

            def weigh(b, u, first=False):
                act.wait_ge(counted, b * NPAIR + u + 1)
                if not (first and u < 4):
                    act.wait_ge(gathered, b * NPAIR + u - 3)
                nc.scalar.activation(wts[:, u % 4], ps_c[:, u % 2], ACT.Relu, bias=BITS0,
                                     scale=-float(EXP_BITS)).then_inc(weighed, 1)

            def collect(b, first):
                act.wait_ge(gathered, (b + 1) * NPAIR)
                if not first:
                    act.wait_ge(add_step, b * 2)
                nc.scalar.copy(agg[:].rearrange("p (h t) d -> p h (t d)", t=2), ps_o[:, :, 0:2 * SP3]).then_inc(agg_ready, 1)

            for u in range(NPAIR):
                weigh(0, u, True)
            weigh(1, 0)
            collect(0, True)
            for u in range(1, NPAIR):
                weigh(1, u)
            with act.Fori(2, NB) as b:
                for u in range(NPAIR):
                    weigh(b, u)
                    if u == 0:
                        collect(b - 1, False)
            collect(NB - 1, False)

        @block.vector
        def _(dve):
            done = [0]

            def link(ins):
                done[0] += 1
                ins.then_inc(ln_step, 1)
                dve.wait_ge(ln_step, done[0])

            def col(k, t0):
                return stat[:, k, t0:t0 + GT]

            def wide(k, t0):
                return stat[:, k, t0:t0 + GT].rearrange("p (t a) -> p t a", a=1).to_broadcast([P, GT, D])

            dve.wait_ge(x_in, 16)
            for g in range(LNG):
                t0 = NT - (g + 1) * GT
                xg, cg, hg = (a[:, t0:t0 + GT, :] for a in (xs, xc, hn))
                link(nc.vector.tensor_reduce(col(0, t0), xg, AX_X, ALU.add))
                link(nc.vector.tensor_scalar(col(1, t0), col(0, t0), 1.0 / D, None, ALU.mult))
                link(nc.vector.tensor_tensor(cg, xg, wide(1, t0), ALU.subtract))
                link(nc.vector.tensor_tensor(hg, cg, cg, ALU.mult))
                link(nc.vector.tensor_reduce(col(0, t0), hg, AX_X, ALU.add))
                nc.vector.tensor_scalar(col(2, t0), col(0, t0), 1.0 / D, EPS, ALU.mult, ALU.add).then_inc(ln_var, 1)
                dve.wait_ge(ln_sqrt, g + 1)
                link(nc.vector.reciprocal(col(4, t0), col(3, t0)))
                link(nc.vector.tensor_tensor(col(0, t0), col(4, t0), col(4, t0), ALU.mult))
                link(nc.vector.tensor_tensor(col(1, t0), col(0, t0), col(2, t0), ALU.mult))
                link(nc.vector.tensor_scalar(col(0, t0), col(1, t0), -0.5, 1.5, ALU.mult, ALU.add))
                link(nc.vector.tensor_tensor(col(5, t0), col(0, t0), col(4, t0), ALU.mult))
                nc.vector.scalar_tensor_tensor(out=hg, in0=cg, scalar=0.0, in1=wide(5, t0), op0=ALU.max,
                                               op1=ALU.mult).then_inc(h_ready, 1)
            for g in range(LNG):
                t0 = NT - (g + 1) * GT
                dve.wait_ge(s_product, g + 1)
                link(nc.vector.tensor_scalar(s_f[:], ps_s, 2.0 ** SHIFT, None, ALU.mult))
                link(nc.vector.tensor_copy(supp[:, t0:t0 + GT, 0, :], s_f[:]))
                link(nc.vector.tensor_tensor(s_r[:], s_f[:], supp[:, t0:t0 + GT, 0, :], ALU.subtract))
                link(nc.vector.tensor_copy(supp[:, t0:t0 + GT, 1, :], s_r[:]))
                link(nc.vector.tensor_tensor(s_f[:], s_r[:], supp[:, t0:t0 + GT, 1, :], ALU.subtract))
                nc.vector.tensor_copy(supp[:, t0:t0 + GT, 2, :], s_f[:]).then_inc(s_ready, 1)

            def pair(b, u, first):
                s, r = b * NPAIR + u, u % 4
                dve.wait_ge(turned, s + 1)
                if not (first and u < 4):
                    dve.wait_ge(counted, s - 3)
                nc.vector.tensor_scalar(mask[:, r], ps_t[:, u % 2], 0.0, None, ALU.not_equal).then_inc(masked, 1)
                dve.wait_ge(masked, s + 1)
                if u >= 1:
                    dve.wait_ge(summed, b * SUMS + 2 * u - 1)
                    nc.vector.tensor_tensor(later[:, r, 1], later[:, r, 0], mask[:, r, 0],
                                            ALU.add).then_inc(summed, 1)
                    dve.wait_ge(summed, b * SUMS + 2 * u)
                if u < NPAIR - 1:
                    before = mask[:, r, 0] if u == 0 else later[:, r, 1]
                    if not (first and u < 3):
                        dve.wait_ge(counted, s - 2)
                    nc.vector.tensor_tensor(later[:, (r + 1) % 4, 0], before, mask[:, r, 1],
                                            ALU.add).then_inc(summed, 1)

            for u in range(NPAIR):
                pair(0, u, True)
            with dve.Fori(1, NB) as b:
                for u in range(NPAIR):
                    pair(b, u, False)

        @block.tensor
        def _(pe):
            pe.wait_ge(consts_step, CONSTS)
            for g in range(LNG):
                t0 = NT - (g + 1) * GT
                pe.wait_ge(h_ready, g + 1)
                if g >= 1:
                    pe.wait_ge(hT_ready, g)
                for t in range(GT):
                    ins = nc.tensor.transpose(ps_h[:, t * P:(t + 1) * P], hn[:, t0 + t, :], ident_f[:])
                ins.then_inc(h_turned, 1)
                pe.wait_ge(hT_ready, g + 1)
                if g == 0:
                    pe.wait_ge(w_in, 16)
                else:
                    pe.wait_ge(s_ready, g)
                for t in range(GT):
                    ins = nc.tensor.matmul(ps_s[:, t, :], hT[:, t * P:(t + 1) * P], wsb[:], start=True, stop=True)
                ins.then_inc(s_product, 1)
            pe.wait_ge(s_ready, LNG)

            def turn(b, u, first):
                s, q = b * NPAIR + u, u // PPP
                if u % PPP == 0:
                    pe.wait_ge(panel_in[q], (b + 1) * 16)
                if not (first and u < 2):
                    pe.wait_ge(masked, s - 1)
                for k in range(2):
                    c = (PPP - 1 - u % PPP) * 2 + (1 - k)
                    for t in range(RT):
                        ins = nc.tensor.transpose(ps_t[:, u % 2, k, t * P:(t + 1) * P],
                                                  panel_hi[:, q, t, c * P:(c + 1) * P], ident[:])
                ins.then_inc(turned, 1)

            def count(b, u, first):
                s, r = b * NPAIR + u, u % 4
                pe.wait_ge(masked, s + 1)
                if u >= 1:
                    pe.wait_ge(summed, b * SUMS + 2 * u)
                if not (first and u < 2):
                    pe.wait_ge(weighed, s - 1)
                for k in range(2):
                    nc.tensor.matmul(ps_c[:, u % 2, k], tri[:], mask[:, r, k], start=True, stop=(u == 0 and k == 0))
                if u >= 1:
                    nc.tensor.matmul(ps_c[:, u % 2, 0], ones[:], later[:, r, 0], start=False, stop=True)
                right = mask[:, r, 0] if u == 0 else later[:, r, 1]
                nc.tensor.matmul(ps_c[:, u % 2, 1], ones[:], right, start=False, stop=True).then_inc(counted, 1)

            def gather(b, u, first):
                s, r = b * NPAIR + u, u % 4
                pe.wait_ge(weighed, s + 1)
                if u == 0 and not first:
                    pe.wait_ge(agg_ready, b)
                for k in range(2):
                    c = NT - 1 - 2 * u - k
                    for t in range(RT):
                        ins = nc.tensor.matmul(ps_o[:, t // 2, t % 2 * SP3:(t % 2 + 1) * SP3], wts_bf[:, r, k, t * P:(t + 1) * P],
                                               supp[:, c, :, :].rearrange("p k d -> p (k d)"),
                                               start=(u == 0 and k == 0 and t % 2 == 0),
                                               stop=(u == NPAIR - 1 and k == 1), skip_group_check=True)
                ins.then_inc(gathered, 1)

            for u in range(NPAIR):
                turn(0, u, True)
                if u >= 1:
                    count(0, u - 1, True)
                if u >= 2:
                    gather(0, u - 2, True)
            with pe.Fori(1, NB) as b:
                for u in range(NPAIR):
                    turn(b, u, False)
                    if u >= 1:
                        count(b, u - 1, False)
                    else:
                        count(b - 1, NPAIR - 1, False)
                    if u >= 2:
                        gather(b, u - 2, False)
                    else:
                        gather(b - 1, NPAIR - 2 + u, False)
            count(NB - 1, NPAIR - 1, False)
            gather(NB - 1, NPAIR - 2, False)
            gather(NB - 1, NPAIR - 1, False)


_INS = ["x", "adj", "L0_gnn_weight", "L0_gnn_bias"]


def kernel(**inputs):
    import numpy as _np
    import concourse.bacc as _bacc
    from concourse import mybir as _mybir
    from concourse.bass_utils import run_bass_kernel_spmd as _run

    nc = _bacc.Bacc("TRN2", target_bir_lowering=False, num_devices=1)
    arrays, args = {}, []
    for name in _INS:
        a = _np.ascontiguousarray(inputs[name])
        arrays[f"in_{name}_dram"] = a
        args.append(nc.dram_tensor(f"in_{name}_dram", a.shape, _mybir.dt.from_np(a.dtype), kind="ExternalInput").ap())
    shape = arrays["in_x_dram"].shape
    args.append(nc.dram_tensor("out_0_dram", shape, _mybir.dt.float32, kind="ExternalOutput").ap())
    gnn_layer(nc, *args)
    r = _run(nc, [arrays], core_ids=[0])
    return r.results[0]["out_0_dram"]
```

```python
from contextlib import ExitStack

import concourse.bass as bass
from concourse import mybir

F32 = mybir.dt.float32
BF16 = mybir.dt.bfloat16
I16 = mybir.dt.int16
ALU = mybir.AluOpType
ACT = mybir.ActivationFunctionType
AX_X = mybir.AxisListType.X


P = 128
RT = 2
W = 124
CARRY = P - W
G3 = 3
PANEL_GROUPS = [3, 3, 3, 2]
PANELS = len(PANEL_GROUPS)
MAX_NEIGH = 100
EPS = 1e-5
EXP_BITS = 128
SHIFT = 127 - MAX_NEIGH
OFF = 8192.0

BITS0 = EXP_BITS * (MAX_NEIGH - OFF)


def gnn_layer(nc, x, adj, weight, bias, out):
    N, D = x.shape
    NT = N // P
    BI = RT * P
    NB = N // BI
    NC = (N - P) // W + 1
    NG = NC // G3
    NQ = NC - 1
    assert NQ * W + P == N and NG * G3 == NC and sum(PANEL_GROUPS) == NG and NQ % CARRY == 0 and NB % 2 == 0
    GW = G3 * W
    PW = max(PANEL_GROUPS) * GW + CARRY
    SP3 = 3 * D
    LAG = 4
    LC = NG + LAG
    LG = LC + 2
    HG = 8
    HGS = NT // HG
    HL = NT // 2
    XB = 4
    PG = HG * P // W
    TOTALS_0 = 8
    TOTALS = {3: (1, 9), 7: (9, 21)}

    group0 = [sum(PANEL_GROUPS[:q]) for q in range(PANELS)]
    panel_of = [q for q in range(PANELS) for _ in range(PANEL_GROUPS[q])]

    adj_v = adj.rearrange("(b t p) c -> b p t c", t=RT, p=P)
    out_v = out.rearrange("(b t p) d -> b p t d", t=RT, p=P)
    x_v = x.rearrange("(t p) d -> p t d", p=P)
    x_runs = x.rearrange("(g p t) d -> g p t d", p=P, t=HG)

    with ExitStack() as ctx:
        def sb(name, shape, dt):
            return ctx.enter_context(nc.sbuf_tensor(name, shape, dt))

        def psum(name, shape, dt):
            return ctx.enter_context(nc.psum_tensor(name, shape, dt))

        def sem(name):
            return ctx.enter_context(nc.semaphore(name))

        panel = sb("panel", [P, 2 * PANELS, RT, PW], F32)
        panel_hi = panel[:].rearrange("p q t c -> p (q t c)").bitcast(BF16).rearrange(
            "p (q t c h) -> p q t c h", q=2 * PANELS, t=RT, h=2)[:, :, :, :, 1]
        mask = sb("mask", [P, 2, NC, BI], BF16)
        right = sb("right", [P, 2, BI], BF16)
        wts = sb("wts", [P, NG, G3, BI], I16)
        wts_bf = wts[:].rearrange("p g k i -> p (g k i)").bitcast(BF16).rearrange(
            "p (g k i) -> p g k i", g=NG, k=G3)
        supp = sb("supp", [P, NC, 3, D], BF16)
        ident = sb("ident", [P, P], BF16)
        ident_f = sb("ident_f", [P, P], F32)
        tri = sb("tri", [P, P], BF16)
        tri_last = sb("tri_last", [P, P], BF16)
        ones = sb("ones", [P, P], BF16)
        left = sb("left", [P, 2 * NQ], BF16)
        wsb = sb("wsb", [D, D], F32)
        bias_sb = sb("bias_sb", [P, D], F32)
        xs = sb("xs", [P, NT, D], F32)
        xb = sb("xb", [P, NT, D], F32)
        xc = sb("xc", [P, NT, D], F32)
        hn = sb("hn", [P, NT, D], F32)
        hT = sb("hT", [D, N], F32)
        xr = sb("xr", [P, NT, D], F32)
        s_r = sb("s_r", [P, 2, PG, D], F32)
        stat = sb("stat", [P, 7, NT], F32)
        agg = sb("agg", [P, RT, SP3], F32)
        part = sb("part", [P, 2, RT, D], F32)
        res = sb("res", [P, RT, D], F32)

        ps_t = psum("ps_t", [P, 2, 1024], BF16)
        ps_c = psum("ps_c", [P, 2, 1024], F32)
        ps_o = psum("ps_o", [P, 512], F32)
        ps_r = psum("ps_r", [P, 512], F32)

        panel_in = [sem(f"panel_in{q}") for q in range(2 * PANELS)]
        xr_in = [sem(f"xr_in{g}") for g in range(HGS)]
        x_in = [sem(f"x_in{g}") for g in range(XB)]
        w_in = sem("w_in")
        bias_in = sem("bias_in")
        consts = sem("consts")
        ln_step = sem("ln_step")
        ln_centred = sem("ln_centred")
        ln_square = sem("ln_square")
        ln_var = sem("ln_var")
        ln_sqrt = sem("ln_sqrt")
        h_ready = sem("h_ready")
        h_turned = sem("h_turned")
        hT_ready = sem("hT_ready")
        s_product = sem("s_product")
        s_high = sem("s_high")
        s_rest = sem("s_rest")
        s_middle = sem("s_middle")
        s_ready = sem("s_ready")
        xb_ready = sem("xb_ready")
        turned = sem("turned")
        masked = sem("masked")
        totalled = sem("totalled")
        right_ready = sem("right_ready")
        right_in = sem("right_in")
        counted = sem("counted")
        weighed = sem("weighed")
        gathered = sem("gathered")
        agg_ready = sem("agg_ready")
        add_step = sem("add_step")
        res_ready = sem("res_ready")
        stored = sem("stored")

        CONSTS = 8
        SUPPORT_AT = (2, 3, 5, 6, 7)
        FEATURES_AT = (1, 1, 3, 3)
        products = [(g * PG, PG) for g in range(HGS)] + [(HGS * PG, NC - HGS * PG)]

        def product(g, n):
            return (ps_r if g % 2 else ps_o)[:, 0:n * D]

        block = ctx.enter_context(nc.Block())

        @block.sync
        def _(sp):
            def load(b, q):
                slot, c0, n = b % 2 * PANELS + q, group0[q] * GW, PANEL_GROUPS[q] * GW + CARRY
                if b >= 2:
                    sp.wait_ge(turned, (b - 2) * NG + group0[q] + PANEL_GROUPS[q])
                before = b * PANELS + q - 2
                if before >= 0:
                    sp.wait_ge(panel_in[before % (2 * PANELS)], (before // (2 * PANELS) + 1) * 16)
                sp.dma_start(panel[:, slot, :, 0:n], adj_v[b, :, :, c0:c0 + n]).then_inc(panel_in[slot], 16)

            def store(b):
                sp.wait_ge(res_ready, b + 1)
                sp.dma_start(out_v[b], res[:]).then_inc(stored, 16)

            for g in range(HGS):
                sp.dma_start(xr[:, g * HG:(g + 1) * HG, :], x_runs[g]).then_inc(xr_in[g], 16)
            for b in range(NB):
                if b % XB == 2:
                    t0, n = b // XB * NT // XB, NT // XB
                    sp.dma_start(xs[:, t0:t0 + n, :], x_v[:, t0:t0 + n, :]).then_inc(x_in[b // XB], 16)
                for q in range(PANELS):
                    load(b, q)
                    if q == 1 and b >= 4:
                        store(b - 4)
            for b in range(NB - 4, NB):
                store(b)
            sp.wait_ge(stored, 16 * NB)

        @block.gpsimd
        def _(pool):
            done = [0]

            def const(ins):
                done[0] += 1
                ins.then_inc(consts, 1)
                pool.wait_ge(consts, done[0])

            def select(dst, src, op, fill, base, step, channel):
                const(nc.gpsimd.affine_select(out=dst, in_=src, compare_op=op, fill=fill, base=base,
                                              pattern=[[step, dst.shape[1]]], channel_multiplier=channel))

            const(nc.gpsimd.memset(ones[:], 1.0))
            select(ident[:], ones[:], ALU.is_equal, 0.0, 0, -1, 1)
            select(tri_last[:], ones[:], ALU.is_gt, 0.0, 0, -1, 1)
            select(tri_last[:], tri_last[:], ALU.not_equal, -OFF, 0, -1, 1)
            select(tri[:], tri_last[:], ALU.is_gt, 0.0, W, -1, 0)
            select(left[:, 0:NQ], ones[:, 0:NQ], ALU.is_gt, 0.0, W, 0, -1)
            const(nc.gpsimd.memset(left[:, NQ:2 * NQ], 0.0))
            select(ident_f[:], ones[:], ALU.is_equal, 0.0, 0, -1, 1)
            pool.dma_start(bias_sb[:], bias.partition_broadcast(P)).then_inc(bias_in, 16)
            pool.wait_ge(bias_in, 16)
            def finish(b, first):
                pool.wait_ge(agg_ready, b + 1)
                nc.gpsimd.tensor_tensor(part[:, 0], agg[:, :, 2 * D:3 * D], agg[:, :, D:2 * D],
                                        ALU.add).then_inc(add_step, 1)
                pool.wait_ge(add_step, b * 2 + 1)
                nc.gpsimd.tensor_tensor(part[:, 1], part[:, 0], agg[:, :, 0:D], ALU.add).then_inc(add_step, 1)
                pool.wait_ge(add_step, b * 2 + 2)
                if not first:
                    pool.wait_ge(stored, b * 16)
                nc.gpsimd.tensor_tensor(res[:], part[:, 1], xb[:, bass.ds(b * RT, RT), :],
                                        ALU.add).then_inc(res_ready, 1)

            for g in range(XB):
                t0, n = g * NT // XB, NT // XB
                pool.wait_ge(x_in[g], 16)
                nc.gpsimd.tensor_tensor(
                    xb[:, t0:t0 + n, :], xs[:, t0:t0 + n, :],
                    bias_sb[:].rearrange("p (a d) -> p a d", a=1).to_broadcast([P, n, D]), ALU.add).then_inc(xb_ready, 1)
                pool.wait_ge(xb_ready, g + 1)
                if g == 0:
                    finish(0, True)
                with pool.Fori(g * NB // XB + (g == 0), (g + 1) * NB // XB) as b:
                    finish(b, False)

        @block.scalar
        def _(act):
            act.dma_start(wsb[:], weight).then_inc(w_in, 16)

            def square(g):
                act.wait_ge(ln_centred, g + 1)
                nc.scalar.activation(hn[:, g * HL:(g + 1) * HL, :], xc[:, g * HL:(g + 1) * HL, :],
                                     ACT.Square).then_inc(ln_square, 1)

            def root(g):
                act.wait_ge(ln_var, g + 1)
                nc.scalar.activation(stat[:, 3, g * HL:(g + 1) * HL], stat[:, 2, g * HL:(g + 1) * HL],
                                     ACT.Sqrt).then_inc(ln_sqrt, 1)

            def copy_h(g):
                act.wait_ge(h_turned, g + 1)
                nc.scalar.copy(hT[:, g * HG * P:(g + 1) * HG * P].rearrange("d (p t) -> d t p", t=HG),
                               ps_c[0:D, g % 2, :].rearrange("d (t p) -> d t p", t=HG)).then_inc(hT_ready, 1)

            def split(g):
                c0, n = products[g]
                act.wait_ge(s_product, g + 1)
                nc.scalar.mul(supp[:, c0:c0 + n, 0, :], product(g, n).rearrange("p (c d) -> p c d", d=D),
                              2.0 ** SHIFT).then_inc(s_high, 1)
                act.wait_ge(s_rest, g + 1)
                nc.scalar.copy(supp[:, c0:c0 + n, 1, :], s_r[:, g % 2, 0:n, :]).then_inc(s_middle, 1)

            square(0)
            square(1)
            root(0)
            root(1)
            copy_h(0)
            copy_h(1)
            split(0)
            copy_h(2)
            copy_h(3)
            for g in range(1, HGS + 1):
                split(g)

            def spread(k, par):
                act.wait_ge(right_ready, k + 1)
                act.dma_start(mask[W:P, par, 0:NQ, :], right[:, par, :]).then_inc(right_in, 16)

            def weigh(k, v, first):
                act.wait_ge(counted, k * NG + v + 1)
                if not first:
                    act.wait_ge(gathered, (k - 1) * NG + v + 1)
                nc.scalar.activation(wts[:, v].rearrange("p k i -> p (k i)"), ps_c[:, (k_par[0] * NG + v) % 2, 0:G3 * BI],
                                     ACT.Relu, bias=BITS0, scale=-float(EXP_BITS)).then_inc(weighed, 1)

            k_par = [0]

            def steps(k, par, n):
                for v in range(NG):
                    if v == 1 and n >= 1:
                        spread(k - 1, 1 - par)
                    j = v - LC % NG
                    back = 1 + (j < 0)
                    if n >= back:
                        k_par[0] = (par + back) % 2
                        weigh(k - back, j % NG, n == back)

            steps(0, 0, 0)
            steps(1, 1, 1)
            steps(2, 0, 2)
            steps(3, 1, 3)
            with act.Fori(2, NB // 2) as m:
                steps(m * 2, 0, 3)
                steps(m * 2 + 1, 1, 3)
            spread(NB - 1, 1)
            for j in range(NG - LC % NG, NG):
                k_par[0] = 0
                weigh(NB - 2, j, False)
            for j in range(NG):
                k_par[0] = 1
                weigh(NB - 1, j, False)

        @block.vector
        def _(dve):
            done = [0]

            def link(ins):
                done[0] += 1
                ins.then_inc(ln_step, 1)
                dve.wait_ge(ln_step, done[0])

            def stage1(k, par, v, n):
                dve.wait_ge(turned, k * NG + v + 1)
                if n >= 2:
                    dve.wait_ge(counted, (k - 2) * NG + v + 1)
                nc.vector.tensor_scalar(mask[:, par, G3 * v:G3 * v + G3, :].rearrange("p k i -> p (k i)"),
                                        ps_t[:, (par * NG + v) % 2, 0:G3 * BI], 0.0, None,
                                        ALU.not_equal).then_inc(masked, 1)

            def take_right(k, par, n):
                dve.wait_ge(totalled, k + 1)
                if n >= 2:
                    dve.wait_ge(right_in, (k - 1) * 16)
                nc.vector.tensor_copy(right[:, par, :], ps_r[:, 0:BI]).then_inc(right_ready, 1)

            def collect(k, n):
                dve.wait_ge(gathered, (k + 1) * NG)
                if n >= 1:
                    dve.wait_ge(add_step, k * 2)
                nc.vector.tensor_copy(agg[:].rearrange("p t d -> p (t d)"), ps_o[:, 0:RT * SP3]).then_inc(agg_ready, 1)

            def steps(k, par, n):
                for v in range(NG):
                    if v == LG % NG and n >= 2:
                        collect(k - 2, n - 2)
                    stage1(k, par, v, n)
                    if v == 0 and n >= 1:
                        take_right(k - 1, 1 - par, n - 1)

            def rows(a, g):
                return a[:, g * HL:(g + 1) * HL, :]

            def col(i, g):
                return stat[:, i, g * HL:(g + 1) * HL]

            def wide(i, g):
                return col(i, g).rearrange("p (t a) -> p t a", a=1).to_broadcast([P, HL, D])

            def centre(g):
                dve.wait_ge(xr_in[2 * g], 16)
                dve.wait_ge(xr_in[2 * g + 1], 16)
                link(nc.vector.tensor_reduce(col(0, g), rows(xr, g), AX_X, ALU.add))
                link(nc.vector.tensor_scalar(col(1, g), col(0, g), 1.0 / D, None, ALU.mult))
                nc.vector.tensor_tensor(rows(xc, g), rows(xr, g), wide(1, g), ALU.subtract).then_inc(ln_centred, 1)

            def variance(g):
                dve.wait_ge(ln_square, g + 1)
                link(nc.vector.tensor_reduce(col(5, g), rows(hn, g), AX_X, ALU.add))
                nc.vector.tensor_scalar(col(2, g), col(5, g), 1.0 / D, EPS, ALU.mult, ALU.add).then_inc(ln_var, 1)

            def normalise(g):
                dve.wait_ge(ln_sqrt, g + 1)
                link(nc.vector.reciprocal(col(4, g), col(3, g)))
                link(nc.vector.tensor_tensor(col(0, g), col(4, g), col(4, g), ALU.mult))
                link(nc.vector.tensor_tensor(col(5, g), col(0, g), col(2, g), ALU.mult))
                link(nc.vector.tensor_scalar(col(0, g), col(5, g), -0.5, 1.5, ALU.mult, ALU.add))
                link(nc.vector.tensor_tensor(col(6, g), col(0, g), col(4, g), ALU.mult))
                nc.vector.scalar_tensor_tensor(out=rows(hn, g), in0=rows(xc, g), scalar=0.0, in1=wide(6, g),
                                               op0=ALU.max, op1=ALU.mult).then_inc(h_ready, 1)

            def split(g):
                c0, n = products[g]
                dve.wait_ge(s_high, g + 1)
                nc.vector.scalar_tensor_tensor(
                    out=s_r[:, g % 2, 0:n, :], in0=product(g, n).rearrange("p (c d) -> p c d", d=D),
                    scalar=2.0 ** SHIFT, in1=supp[:, c0:c0 + n, 0, :], op0=ALU.mult,
                    op1=ALU.subtract).then_inc(s_rest, 1)
                dve.wait_ge(s_middle, g + 1)
                nc.vector.tensor_tensor(supp[:, c0:c0 + n, 2, :], s_r[:, g % 2, 0:n, :], supp[:, c0:c0 + n, 1, :],
                                        ALU.subtract).then_inc(s_ready, 1)

            centre(0)
            centre(1)
            variance(0)
            normalise(0)
            variance(1)
            stage1(0, 0, 0, 0)
            normalise(1)
            stage1(0, 0, 1, 0)
            for v in range(2, NG):
                stage1(0, 0, v, 0)
                if v in SUPPORT_AT:
                    split(SUPPORT_AT.index(v))
            steps(1, 1, 1)
            steps(2, 0, 2)
            steps(3, 1, 3)
            with dve.Fori(2, NB // 2) as m:
                steps(m * 2, 0, 4)
                steps(m * 2 + 1, 1, 4)
            take_right(NB - 1, 1, 3)
            collect(NB - 2, 3)
            collect(NB - 1, 3)

        @block.tensor
        def _(pe):
            def turn(k, par, v, n):
                q = panel_of[v]
                slot = par * PANELS + q
                if v == group0[q]:
                    pe.wait_ge(panel_in[slot], (k // 2 + 1) * 16 if isinstance(k, int) else (k_half[0] + 1) * 16)
                if n >= 1 or v >= 2:
                    pe.wait_ge(masked, k * NG + v - 1)
                for i in range(G3):
                    c = (v - group0[q]) * G3 + i
                    for t in range(RT):
                        ins = nc.tensor.transpose(ps_t[:, (par * NG + v) % 2, (i * RT + t) * P:(i * RT + t + 1) * P],
                                                  panel_hi[:, slot, t, c * W:c * W + P], ident[:])
                ins.then_inc(turned, 1)

            def totals(k, par, c0, c1, n):
                pe.wait_ge(masked, k * NG + (c1 - 1) // G3 + 1)
                if c0 == 1 and n >= 1:
                    pe.wait_ge(right_ready, k)
                if n == 0:
                    pe.wait_ge(s_rest, HGS + 1)
                for c in range(c0, c1):
                    r = c % CARRY * NQ
                    ones_left = ones[:, 0:NQ] if c == NQ else left[:, NQ - c:2 * NQ - c]
                    ins = nc.tensor.matmul(ps_r[r:r + NQ, 0:BI], ones_left, mask[:, par, c, :],
                                           start=(c <= CARRY), stop=(c > NQ - CARRY))
                if c1 == NC:
                    ins.then_inc(totalled, 1)

            def count(k, par, v):
                if v == 0:
                    pe.wait_ge(right_in, (k + 1) * 16)
                if not (isinstance(k, int) and k == 0 and v < 2):
                    pe.wait_ge(weighed, k * NG + v - 1)
                c, out_c = G3 * v, ps_c[:, (par * NG + v) % 2, :]
                flat = mask[:, par, c:c + G3, :].rearrange("p k i -> p (k i)")
                nc.tensor.matmul(out_c[:, 0:2 * BI], tri[:], flat[:, 0:2 * BI], start=True, stop=True)
                nc.tensor.matmul(out_c[:, 2 * BI:3 * BI], tri_last[:] if v == NG - 1 else tri[:],
                                 flat[:, 2 * BI:3 * BI], start=True, stop=True).then_inc(counted, 1)

            def gather(k, par, v, n):
                pe.wait_ge(weighed, k * NG + v + 1)
                if v == 0 and n >= 1:
                    pe.wait_ge(agg_ready, k)
                if n == 0 and k == 0:
                    pe.wait_ge(s_ready, min((G3 * v + G3 - 1) // PG, HGS) + 1)
                for i in range(G3):
                    c = G3 * v + i
                    for t in range(RT):
                        ins = nc.tensor.matmul(ps_o[:, t * SP3:(t + 1) * SP3], wts_bf[:, v, i, t * P:(t + 1) * P],
                                               supp[:, c, :, :].rearrange("p k d -> p (k d)"),
                                               start=(c == 0 and t == 0), stop=(c == NC - 1),
                                               skip_group_check=True)
                ins.then_inc(gathered, 1)

            k_half = [0]

            def stage2(k, par, n, v):
                for lag, what in ((LC, "count"), (LG, "gather")):
                    j = v - lag % NG
                    back = lag // NG + (j < 0)
                    if n < back:
                        continue
                    if what == "count":
                        count(k - back, (par + back) % 2, j % NG)
                    else:
                        gather(k - back, (par + back) % 2, j % NG, n - back)

            def features(g):
                pe.wait_ge(h_ready, g * HG // HL + 1)
                if g >= 2:
                    pe.wait_ge(hT_ready, g - 1)
                for t in range(HG):
                    ins = nc.tensor.transpose(ps_c[0:D, g % 2, t * P:(t + 1) * P], hn[:, g * HG + t, :], ident_f[:])
                ins.then_inc(h_turned, 1)

            def support(g):
                c0, n = products[g]
                if g < HGS:
                    pe.wait_ge(hT_ready, g + 1)
                if g == 0:
                    pe.wait_ge(w_in, 16)
                if g >= 2:
                    pe.wait_ge(s_rest, g - 1)
                for i in range(n):
                    ins = nc.tensor.matmul(product(g, n)[:, i * D:(i + 1) * D], hT[:, (c0 + i) * W:(c0 + i) * W + P], wsb[:],
                                           start=True, stop=True)
                ins.then_inc(s_product, 1)

            def steps(k, par, n):
                for v in range(NG):
                    turn(k, par, v, n)
                    if n == 0:
                        prologue(v)
                    if v == 0 and n >= 1:
                        totals(k - 1, 1 - par, 21, NC, n - 1)
                    if v in TOTALS and n >= 1:
                        totals(k, par, *TOTALS[v], n)
                    if n == 0 and v == TOTALS_0:
                        totals(k, par, 1, 21, 0)
                    stage2(k, par, n, v)

            def prologue(v):
                for g in range(HGS):
                    if FEATURES_AT[g] == v:
                        features(g)
                for g in range(HGS + 1):
                    if SUPPORT_AT[g] == v:
                        support(g)

            pe.wait_ge(consts, CONSTS)
            steps(0, 0, 0)
            steps(1, 1, 1)
            steps(2, 0, 2)
            steps(3, 1, 3)
            with pe.Fori(2, NB // 2) as m:
                k_half[0] = m
                steps(m * 2, 0, 4)
                steps(m * 2 + 1, 1, 4)
            totals(NB - 1, 1, 21, NC, 3)
            for v in range(LG):
                if v < LC:
                    j = v - LC % NG
                    count(NB - 1 - (j < 0), 1 - (j < 0), j % NG)
                j = v - LG % NG
                gather(NB - 1 - (j < 0), 1 - (j < 0), j % NG, 3)


_INS = ["x", "adj", "L0_gnn_weight", "L0_gnn_bias"]


def kernel(**inputs):
    import numpy as _np
    import concourse.bacc as _bacc
    from concourse import mybir as _mybir
    from concourse.bass_utils import run_bass_kernel_spmd as _run

    nc = _bacc.Bacc("TRN2", target_bir_lowering=False, num_devices=1)
    arrays, args = {}, []
    for name in _INS:
        a = _np.ascontiguousarray(inputs[name])
        arrays[f"in_{name}_dram"] = a
        args.append(nc.dram_tensor(f"in_{name}_dram", a.shape, _mybir.dt.from_np(a.dtype), kind="ExternalInput").ap())
    shape = arrays["in_x_dram"].shape
    args.append(nc.dram_tensor("out_0_dram", shape, _mybir.dt.float32, kind="ExternalOutput").ap())
    gnn_layer(nc, *args)
    r = _run(nc, [arrays], core_ids=[0])
    return r.results[0]["out_0_dram"]
```

```python
from contextlib import ExitStack

import concourse.bass as bass
from concourse import mybir

F32 = mybir.dt.float32
BF16 = mybir.dt.bfloat16
I16 = mybir.dt.int16
ALU = mybir.AluOpType
ACT = mybir.ActivationFunctionType
AX_X = mybir.AxisListType.X


P = 128
RT = 2
W = 124
CARRY = P - W
G3 = 3
PANEL_GROUPS = [2, 2, 2, 2, 2, 1]
PANELS = len(PANEL_GROUPS)
MAX_NEIGH = 100
EPS = 1e-5
EXP_BITS = 128
SHIFT = 127 - MAX_NEIGH
OFF = 8192.0

BITS0 = EXP_BITS * (MAX_NEIGH - OFF)


def gnn_layer(nc, x, adj, weight, bias, out):
    N, D = x.shape
    NT = N // P
    BI = RT * P
    NB = N // BI
    NC = (N - P) // W + 1
    NG = NC // G3
    NQ = NC - 1
    assert NQ * W + P == N and NG * G3 == NC and sum(PANEL_GROUPS) == NG and NQ % CARRY == 0 and NB % 2 == 0
    GW = G3 * W
    PW = max(PANEL_GROUPS) * GW + CARRY
    SP3 = 3 * D
    LAG = 5
    LC = NG + LAG
    LG = LC + 2
    KP = NQ // 2
    HALF = KP * W
    ST = KP + 1
    LN = [(0, KP // 2), (KP // 2, ST)]
    RUN = KP // 2
    XB = 4
    TOTALS = {3: (1, 9), 7: (9, 17)}
    TOTALS_REST = 17

    group0 = [sum(PANEL_GROUPS[:q]) for q in range(PANELS)]
    panel_of = [q for q in range(PANELS) for _ in range(PANEL_GROUPS[q])]

    adj_v = adj.rearrange("(b t p) c -> b p t c", t=RT, p=P)
    out_v = out.rearrange("(b t p) d -> b p t d", t=RT, p=P)
    x_v = x.rearrange("(t p) d -> p t d", p=P)

    with ExitStack() as ctx:
        def sb(name, shape, dt):
            return ctx.enter_context(nc.sbuf_tensor(name, shape, dt))

        def psum(name, shape, dt):
            return ctx.enter_context(nc.psum_tensor(name, shape, dt))

        def sem(name):
            return ctx.enter_context(nc.semaphore(name))

        panel = sb("panel", [P, 2 * PANELS, RT, PW], F32)
        panel_hi = panel[:].rearrange("p q t c -> p (q t c)").bitcast(BF16).rearrange(
            "p (q t c h) -> p q t c h", q=2 * PANELS, t=RT, h=2)[:, :, :, :, 1]
        mask = sb("mask", [P, 2, NC, BI], BF16)
        right = sb("right", [P, 2, BI], BF16)
        wts = sb("wts", [P, NG, G3, BI], I16)
        wts_bf = wts[:].rearrange("p g k i -> p (g k i)").bitcast(BF16).rearrange(
            "p (g k i) -> p g k i", g=NG, k=G3)
        supp = sb("supp", [P, NC, 3, D], BF16)
        ident = sb("ident", [P, P], BF16)
        ident_f = sb("ident_f", [P, P], F32)
        tri = sb("tri", [P, P], BF16)
        tri_last = sb("tri_last", [P, P], BF16)
        ones = sb("ones", [P, P], BF16)
        left = sb("left", [P, 2 * NQ], BF16)
        wsb = sb("wsb", [P, 2, D], F32)
        bias_sb = sb("bias_sb", [P, D], F32)
        xs = sb("xs", [P, NT, D], F32)
        xb = sb("xb", [P, NT, D], F32)
        xr = sb("xr", [P, 2, ST, D], F32)
        xc = sb("xc", [P, 2, ST, D], F32)
        sq = sb("sq", [P, 2, ST, D], F32)
        hn = sb("hn", [P, ST, 2, D], F32)
        hT = sb("hT", [P, ST, P], F32)
        s_r = sb("s_r", [P, 2, RUN, 2, D], F32)
        stat = sb("stat", [P, 7, 2, ST], F32)
        root_of_0 = sb("root_of_0", [D, 1], F32)
        agg = sb("agg", [P, RT, D], F32)
        res = sb("res", [P, RT, D], F32)

        ps_t = psum("ps_t", [P, 2, 1024], BF16)
        ps_c = psum("ps_c", [P, 2, 1024], F32)
        ps_o = psum("ps_o", [P, 512], F32)
        ps_r = psum("ps_r", [P, 512], F32)

        panel_in = [sem(f"panel_in{q}") for q in range(2 * PANELS)]
        xr_in = [sem(f"xr_in{g}") for g in range(2)]
        w_zero = sem("w_zero")
        x_in = [sem(f"x_in{g}") for g in range(XB)]
        w_in = sem("w_in")
        bias_in = sem("bias_in")
        consts = sem("consts")
        ln_step = sem("ln_step")
        ln_centred = sem("ln_centred")
        ln_mean = sem("ln_mean")
        ln_square = sem("ln_square")
        ln_var = sem("ln_var")
        ln_sqrt = sem("ln_sqrt")
        h_ready = sem("h_ready")
        h_turned = sem("h_turned")
        hT_ready = sem("hT_ready")
        s_product = sem("s_product")
        s_high = sem("s_high")
        s_rest = sem("s_rest")
        s_middle = sem("s_middle")
        s_ready = sem("s_ready")
        xb_ready = sem("xb_ready")
        turned = sem("turned")
        masked = sem("masked")
        totalled = sem("totalled")
        right_ready = sem("right_ready")
        right_in = sem("right_in")
        counted = sem("counted")
        weighed = sem("weighed")
        gathered = sem("gathered")
        agg_ready = sem("agg_ready")
        res_ready = sem("res_ready")
        stored = sem("stored")

        CONSTS = 8
        WARM = (80, 50, 20)
        FEATURES_AT = (1, 1)
        SUPPORT_AT = (4, 8, 9)
        REST_AT = (8, 11, 12)
        products = [(0, RUN), (RUN, RUN), (KP, 1)]

        def product(g):
            n = products[g][1]
            bank = ps_o[:, P:2 * P] if g == 2 else ps_c[:, g, :]
            return bank.rearrange("p (k a d) -> p k a d", a=2, d=D)[:, 0:n]

        def supp_part(g, i):
            k0, n = products[g]
            if g == 2:
                return supp[:, KP:NC:KP, i, :].rearrange("p (k a) d -> p k a d", k=1)
            return supp[:, 0:NQ, i, :].rearrange("p (a k) d -> p k a d", a=2)[:, k0:k0 + n]

        block = ctx.enter_context(nc.Block())

        @block.sync
        def _(sp):
            def load(b, q):
                slot, c0, n = b % 2 * PANELS + q, group0[q] * GW, PANEL_GROUPS[q] * GW + CARRY
                if b >= 2:
                    sp.wait_ge(turned, (b - 2) * NG + group0[q] + PANEL_GROUPS[q])
                if b == 2 and q == 0:
                    sp.wait_ge(right_ready, 1)
                    sp.dma_start(mask[W:P, 0, 0:NQ, :], right[:, 0, :]).then_inc(right_in, 16)
                before = b * PANELS + q - 2
                if before >= 0:
                    sp.wait_ge(panel_in[before % (2 * PANELS)], (before // (2 * PANELS) + 1) * 16)
                sp.dma_start(panel[:, slot, :, 0:n], adj_v[b, :, :, c0:c0 + n]).then_inc(panel_in[slot], 16)

            def store(b):
                sp.wait_ge(res_ready, b + 1)
                sp.dma_start(out_v[b], res[:]).then_inc(stored, 16)

            for g in range(2):
                for a in range(2):
                    r0 = a * HALF + g * RUN * P
                    sp.dma_start(xr[:, a, g * RUN:(g + 1) * RUN, :],
                                 x[r0:r0 + RUN * P, :].rearrange("(p t) d -> p t d", p=P)).then_inc(xr_in[g], 16)
                    if g == 1:
                        r0 = (a + 1) * HALF
                        sp.dma_start(xr[:, a, KP, :], x[r0:r0 + P, :]).then_inc(xr_in[g], 16)
            for b in range(NB):
                if b % XB == 2:
                    t0, n = b // XB * NT // XB, NT // XB
                    sp.dma_start(xs[:, t0:t0 + n, :], x_v[:, t0:t0 + n, :]).then_inc(x_in[b // XB], 16)
                for q in range(PANELS):
                    load(b, q)
                    if q == 1 and b >= 4:
                        store(b - 4)
            for b in range(NB - 4, NB):
                store(b)
            sp.wait_ge(stored, 16 * NB)

        @block.gpsimd
        def _(pool):
            done = [0]

            def const(ins):
                done[0] += 1
                ins.then_inc(consts, 1)
                pool.wait_ge(consts, done[0])

            def select(dst, src, op, fill, base, step, channel):
                const(nc.gpsimd.affine_select(out=dst, in_=src, compare_op=op, fill=fill, base=base,
                                              pattern=[[step, dst.shape[1]]], channel_multiplier=channel))

            const(nc.gpsimd.memset(ones[:], 1.0))
            select(ident[:], ones[:], ALU.is_equal, 0.0, 0, -1, 1)
            select(tri_last[:], ones[:], ALU.is_gt, 0.0, 0, -1, 1)
            select(tri_last[:], tri_last[:], ALU.not_equal, -OFF, 0, -1, 1)
            select(tri[:], tri_last[:], ALU.is_gt, 0.0, W, -1, 0)
            select(left[:, 0:NQ], ones[:, 0:NQ], ALU.is_gt, 0.0, W, 0, -1)
            const(nc.gpsimd.memset(left[:, NQ:2 * NQ], 0.0))
            select(ident_f[:], ones[:], ALU.is_equal, 0.0, 0, -1, 1)
            t0, t1 = LN[1]
            pool.wait_ge(ln_mean, 1)
            nc.gpsimd.tensor_tensor(
                xc[:, 1, t0:t1, :], xr[:, 1, t0:t1, :],
                stat[:, 1, 1, t0:t1].rearrange("p (t e) -> p t e", e=1).to_broadcast([P, t1 - t0, D]),
                ALU.subtract).then_inc(ln_centred, 1)
            pool.dma_start(bias_sb[:], bias.partition_broadcast(P)).then_inc(bias_in, 16)

            def finish(b, first):
                pool.wait_ge(agg_ready, b + 1)
                if not first:
                    pool.wait_ge(stored, b * 16)
                nc.gpsimd.tensor_tensor(res[:], agg[:], xb[:, bass.ds(b * RT, RT), :],
                                        ALU.add).then_inc(res_ready, 1)

            for g in range(3):
                pool.wait_ge(s_middle, g + 1)
                nc.gpsimd.tensor_tensor(supp_part(g, 2), s_r[:, g % 2, 0:products[g][1]], supp_part(g, 1),
                                        ALU.subtract).then_inc(s_ready, 1)

            pool.wait_ge(bias_in, 16)
            for g in range(XB):
                t0, n = g * NT // XB, NT // XB
                pool.wait_ge(x_in[g], 16)
                nc.gpsimd.tensor_tensor(
                    xb[:, t0:t0 + n, :], xs[:, t0:t0 + n, :],
                    bias_sb[:].rearrange("p (a d) -> p a d", a=1).to_broadcast([P, n, D]),
                    ALU.add).then_inc(xb_ready, 1)
                pool.wait_ge(xb_ready, g + 1)
                if g == 0:
                    finish(0, True)
                with pool.Fori(g * NB // XB + (g == 0), (g + 1) * NB // XB) as b:
                    finish(b, False)

        @block.scalar
        def _(act):
            act.wait_ge(w_zero, 1)
            act.dma_start(wsb[0:D, 0, :], weight).then_inc(w_in, 16)
            act.dma_start(wsb[D:P, 1, :], weight).then_inc(w_in, 16)
            nc.scalar.activation(root_of_0[:], wsb[:, 1, 0:1][0:D], ACT.Sqrt)

            def square(g):
                t0, t1 = LN[g]
                act.wait_ge(ln_centred, 1 + 2 * g)
                nc.scalar.activation(sq[:, :, t0:t1, :], xc[:, :, t0:t1, :], ACT.Square).then_inc(ln_square, 1)

            def root(g):
                t0, t1 = LN[g]
                act.wait_ge(ln_var, g + 1)
                nc.scalar.activation(stat[:, 3, :, t0:t1], stat[:, 2, :, t0:t1], ACT.Sqrt).then_inc(ln_sqrt, 1)

            def copy_h(g):
                act.wait_ge(h_turned, g + 1)
                t0 = g * RUN
                nc.scalar.copy(hT[:, t0:t0 + RUN, :].rearrange("d t p -> d (t p)").rearrange("d (p t) -> d t p", t=RUN),
                               ps_c[:, g, :].rearrange("d (t p) -> d t p", t=RUN)).then_inc(hT_ready, 1)
                if g == 1:
                    nc.scalar.copy(hT[:, KP, :], ps_o[:, 0:P]).then_inc(hT_ready, 1)

            def high(g):
                act.wait_ge(s_product, g + 1)
                nc.scalar.mul(supp_part(g, 0), product(g), 2.0 ** SHIFT).then_inc(s_high, 1)

            def middle(g):
                n = products[g][1]
                act.wait_ge(s_rest, 2 * (g + 1))
                nc.scalar.copy(supp_part(g, 1), s_r[:, g % 2, 0:n]).then_inc(s_middle, 1)

            def spread(k, par):
                act.wait_ge(right_ready, k + 1)
                act.dma_start(mask[W:P, par, 0:NQ, :], right[:, par, :]).then_inc(right_in, 16)

            square(0)
            root(0)
            square(1)
            root(1)
            copy_h(0)
            copy_h(1)
            high(0)
            high(1)
            middle(0)
            high(2)
            middle(1)
            middle(2)

            def weigh(k, par, v, first):
                act.wait_ge(counted, k * NG + v + 1)
                if not first:
                    act.wait_ge(gathered, (k - 1) * NG + v + 1)
                nc.scalar.activation(wts[:, v].rearrange("p k i -> p (k i)"), ps_c[:, (par * NG + v) % 2, 0:G3 * BI],
                                     ACT.Relu, bias=BITS0, scale=-float(EXP_BITS)).then_inc(weighed, 1)

            def steps(k, par, n):
                for v in range(NG):
                    if v == 1 and n >= 2:
                        spread(k - 1, 1 - par)
                    j = v - LC % NG
                    back = 1 + (j < 0)
                    if n >= back:
                        weigh(k - back, (par + back) % 2, j % NG, n == back)

            steps(0, 0, 0)
            steps(1, 1, 1)
            steps(2, 0, 2)
            steps(3, 1, 3)
            with act.Fori(2, NB // 2) as m:
                steps(m * 2, 0, 3)
                steps(m * 2 + 1, 1, 3)
            spread(NB - 1, 1)
            for j in range(NG - LC % NG, NG):
                weigh(NB - 2, 0, j, False)
            for j in range(NG):
                weigh(NB - 1, 1, j, False)

        @block.vector
        def _(dve):
            done = [0]

            def link(ins):
                done[0] += 1
                ins.then_inc(ln_step, 1)
                dve.wait_ge(ln_step, done[0])

            def stage1(k, par, v, n):
                dve.wait_ge(turned, k * NG + v + 1)
                if n >= 2:
                    dve.wait_ge(counted, (k - 2) * NG + v + 1)
                nc.vector.tensor_scalar(mask[:, par, G3 * v:G3 * v + G3, :].rearrange("p k i -> p (k i)"),
                                        ps_t[:, (par * NG + v) % 2, 0:G3 * BI], 0.0, None,
                                        ALU.not_equal).then_inc(masked, 1)

            def take_right(k, par, n):
                dve.wait_ge(totalled, k + 1)
                if n >= 2:
                    dve.wait_ge(right_in, (k - 1) * 16)
                nc.vector.tensor_copy(right[:, par, :], ps_r[:, 0:BI]).then_inc(right_ready, 1)

            def collect(k, n):
                dve.wait_ge(gathered, (k + 1) * NG)
                if n >= 1:
                    dve.wait_ge(res_ready, k)
                for t in range(RT):
                    ins = nc.vector.tensor_reduce(
                        agg[:, t, :], ps_o[:, t * SP3:(t + 1) * SP3].rearrange("p (i d) -> p d i", i=3), AX_X, ALU.add)
                ins.then_inc(agg_ready, 1)

            def rest_after(step):
                for g in range(3):
                    if REST_AT[g] == step:
                        rest(g)

            def steps(k, par, n):
                for v in range(NG):
                    if v == LG % NG and n >= 2:
                        collect(k - 2, n - 2)
                    stage1(k, par, v, n)
                    if v == 0 and n >= 1:
                        take_right(k - 1, 1 - par, n - 1)
                    if n == 1:
                        rest_after(NG + v)

            def rows(a, g):
                return a[:, :, LN[g][0]:LN[g][1], :]

            def col(i, g):
                return stat[:, i, :, LN[g][0]:LN[g][1]]

            def wide(i, g):
                t0, t1 = LN[g]
                return col(i, g).rearrange("p a (t e) -> p a t e", e=1).to_broadcast([P, 2, t1 - t0, D])

            def centre(g):
                dve.wait_ge(xr_in[g], 32 * (g + 1))
                link(nc.vector.tensor_reduce(col(0, g), rows(xr, g), AX_X, ALU.add))
                mean = nc.vector.tensor_scalar(col(1, g), col(0, g), 1.0 / D, None, ALU.mult)
                if g == 1:
                    mean.then_inc(ln_mean, 1)
                else:
                    link(mean)
                    nc.vector.tensor_tensor(rows(xc, g), rows(xr, g), wide(1, g), ALU.subtract).then_inc(ln_centred, 1)

            def variance(g):
                dve.wait_ge(ln_square, g + 1)
                link(nc.vector.tensor_reduce(col(5, g), rows(sq, g), AX_X, ALU.add))
                nc.vector.tensor_scalar(col(2, g), col(5, g), 1.0 / D, EPS, ALU.mult, ALU.add).then_inc(ln_var, 1)

            def normalise(g):
                dve.wait_ge(ln_sqrt, g + 1)
                link(nc.vector.reciprocal(col(4, g), col(3, g)))
                link(nc.vector.tensor_tensor(col(0, g), col(4, g), col(4, g), ALU.mult))
                link(nc.vector.tensor_tensor(col(5, g), col(0, g), col(2, g), ALU.mult))
                link(nc.vector.tensor_scalar(col(0, g), col(5, g), -0.5, 1.5, ALU.mult, ALU.add))
                link(nc.vector.tensor_tensor(col(6, g), col(0, g), col(4, g), ALU.mult))
                for a in range(2):
                    nc.vector.scalar_tensor_tensor(
                        out=hn[:, LN[g][0]:LN[g][1], a, :], in0=rows(xc, g)[:, a], scalar=0.0, in1=wide(6, g)[:, a],
                        op0=ALU.max, op1=ALU.mult).then_inc(h_ready, 1)

            def rest(g):
                n = products[g][1]
                dve.wait_ge(s_high, g + 1)
                if g == 2:
                    dve.wait_ge(s_ready, 1)
                for a in range(2):
                    nc.vector.scalar_tensor_tensor(out=s_r[:, g % 2, 0:n, a], in0=product(g)[:, :, a],
                                                   scalar=2.0 ** SHIFT, in1=supp_part(g, 0)[:, :, a], op0=ALU.mult,
                                                   op1=ALU.subtract).then_inc(s_rest, 1)

            nc.vector.memset(wsb[:], 0.0).then_inc(w_zero, 1)
            centre(0)
            centre(1)
            variance(0)
            dve.wait_ge(ln_mean, 1)
            nc.vector.tensor_tensor(rows(xc, 1)[:, 0], rows(xr, 1)[:, 0], wide(1, 1)[:, 0],
                                    ALU.subtract).then_inc(ln_centred, 1)
            normalise(0)
            variance(1)
            normalise(1)
            for v in range(NG):
                stage1(0, 0, v, 0)
                rest_after(v)
            steps(1, 1, 1)
            steps(2, 0, 2)
            steps(3, 1, 3)
            with dve.Fori(2, NB // 2) as m:
                steps(m * 2, 0, 4)
                steps(m * 2 + 1, 1, 4)
            take_right(NB - 1, 1, 3)
            collect(NB - 2, 3)
            collect(NB - 1, 3)

        @block.tensor
        def _(pe):
            def turn(k, pair, par, v, n):
                q = panel_of[v]
                slot = par * PANELS + q
                if v == group0[q]:
                    pe.wait_ge(panel_in[slot], (pair + 1) * 16)
                if n >= 1 or v >= 2:
                    pe.wait_ge(masked, k * NG + v - 1)
                for i in range(G3):
                    c = (v - group0[q]) * G3 + i
                    for t in range(RT):
                        ins = nc.tensor.transpose(ps_t[:, (par * NG + v) % 2, (i * RT + t) * P:(i * RT + t + 1) * P],
                                                  panel_hi[:, slot, t, c * W:c * W + P], ident[:])
                ins.then_inc(turned, 1)

            def totals(k, par, c0, c1, n):
                pe.wait_ge(masked, k * NG + (c1 - 1) // G3 + 1)
                if c0 == 1 and n >= 1:
                    pe.wait_ge(right_ready, k)
                for c in range(c0, c1):
                    r = c % CARRY * NQ
                    ones_left = ones[:, 0:NQ] if c == NQ else left[:, NQ - c:2 * NQ - c]
                    ins = nc.tensor.matmul(ps_r[r:r + NQ, 0:BI], ones_left, mask[:, par, c, :],
                                           start=(c <= CARRY), stop=(c > NQ - CARRY))
                if c1 == NC:
                    ins.then_inc(totalled, 1)

            def count(k, par, v, n):
                if v == 0:
                    pe.wait_ge(right_in, (k + 1) * 16)
                if n >= 1 or v >= 2:
                    pe.wait_ge(weighed, k * NG + v - 1)
                if n == 0 and v == 0:
                    pe.wait_ge(s_rest, 6)
                c, out_c = G3 * v, ps_c[:, (par * NG + v) % 2, :]
                flat = mask[:, par, c:c + G3, :].rearrange("p k i -> p (k i)")
                nc.tensor.matmul(out_c[:, 0:2 * BI], tri[:], flat[:, 0:2 * BI], start=True, stop=True)
                nc.tensor.matmul(out_c[:, 2 * BI:3 * BI], tri_last[:] if v == NG - 1 else tri[:],
                                 flat[:, 2 * BI:3 * BI], start=True, stop=True).then_inc(counted, 1)

            def gather(k, par, v, n):
                pe.wait_ge(weighed, k * NG + v + 1)
                if v == 0 and n >= 1:
                    pe.wait_ge(agg_ready, k)
                if n == 0:
                    pe.wait_ge(s_ready, 1 if G3 * (v + 1) <= RUN else 3)
                for i in range(G3):
                    c = G3 * v + i
                    for t in range(RT):
                        ins = nc.tensor.matmul(ps_o[:, t * SP3:(t + 1) * SP3], wts_bf[:, v, i, t * P:(t + 1) * P],
                                               supp[:, c, :, :].rearrange("p k d -> p (k d)"),
                                               start=(c == 0 and t == 0), stop=(c == NC - 1),
                                               skip_group_check=True)
                ins.then_inc(gathered, 1)

            def stage2(k, par, n, v):
                for lag, what in ((LC, "count"), (LG, "gather")):
                    j = v - lag % NG
                    back = lag // NG + (j < 0)
                    if n < back:
                        continue
                    if what == "count":
                        count(k - back, (par + back) % 2, j % NG, n - back)
                    else:
                        gather(k - back, (par + back) % 2, j % NG, n - back)

            def features(g):
                pe.wait_ge(h_ready, 2 * (g + 1))
                for t in range(RUN):
                    ins = nc.tensor.transpose(ps_c[:, g, t * P:(t + 1) * P],
                                              hn[:, g * RUN + t, :, :].rearrange("p a d -> p (a d)"), ident_f[:])
                if g == 1:
                    ins = nc.tensor.transpose(ps_o[:, 0:P], hn[:, KP, :, :].rearrange("p a d -> p (a d)"), ident_f[:])
                ins.then_inc(h_turned, 1)

            def support(g):
                k0, n = products[g]
                pe.wait_ge(hT_ready, min(2 * g + 1, 3))
                if g == 0:
                    pe.wait_ge(w_in, 32)
                flat = hT[:].rearrange("d t p -> d (t p)")
                for i in range(n):
                    r = KP * P if g == 2 else (k0 + i) * W
                    ins = nc.tensor.matmul(product(g)[:, i].rearrange("p a d -> p (a d)"), flat[:, r:r + P],
                                           wsb[:].rearrange("p a d -> p (a d)"), start=True, stop=True)
                ins.then_inc(s_product, 1)

            def steps(k, pair, par, n):
                for v in range(NG):
                    turn(k, pair, par, v, n)
                    if n <= 1:
                        prologue(n * NG + v)
                    if v == 0 and n >= 1:
                        totals(k - 1, 1 - par, TOTALS_REST, NC, n - 1)
                    if v in TOTALS:
                        totals(k, par, *TOTALS[v], n)
                    stage2(k, par, n, v)

            def prologue(step):
                for g in range(2):
                    if FEATURES_AT[g] == step:
                        warm_up(WARM[1 + g])
                        features(g)
                for g in range(3):
                    if SUPPORT_AT[g] == step:
                        support(g)

            def warm_up(n):
                for _ in range(n):
                    nc.tensor.matmul(ps_r[:, BI:BI + P], ident[:], ones[:], start=True, stop=True)

            pe.wait_ge(consts, CONSTS)
            warm_up(WARM[0])
            steps(0, 0, 0, 0)
            steps(1, 0, 1, 1)
            steps(2, 1, 0, 2)
            steps(3, 1, 1, 3)
            with pe.Fori(2, NB // 2) as m:
                steps(m * 2, m, 0, 4)
                steps(m * 2 + 1, m, 1, 4)
            totals(NB - 1, 1, TOTALS_REST, NC, 3)
            for v in range(LG):
                if v < LC:
                    j = v - LC % NG
                    count(NB - 1 - (j < 0), 1 - (j < 0), j % NG, 3)
                j = v - LG % NG
                gather(NB - 1 - (j < 0), 1 - (j < 0), j % NG, 3)


_INS = ["x", "adj", "L0_gnn_weight", "L0_gnn_bias"]


def kernel(**inputs):
    import numpy as _np
    import concourse.bacc as _bacc
    from concourse import mybir as _mybir
    from concourse.bass_utils import run_bass_kernel_spmd as _run

    nc = _bacc.Bacc("TRN2", target_bir_lowering=False, num_devices=1)
    arrays, args = {}, []
    for name in _INS:
        a = _np.ascontiguousarray(inputs[name])
        arrays[f"in_{name}_dram"] = a
        args.append(nc.dram_tensor(f"in_{name}_dram", a.shape, _mybir.dt.from_np(a.dtype), kind="ExternalInput").ap())
    shape = arrays["in_x_dram"].shape
    args.append(nc.dram_tensor("out_0_dram", shape, _mybir.dt.float32, kind="ExternalOutput").ap())
    gnn_layer(nc, *args)
    r = _run(nc, [arrays], core_ids=[0])
    return r.results[0]["out_0_dram"]
```
